# Optimizing a Trainium2 kernel written in Bass

```python
import numpy as np
import jax
import jax.numpy as jnp

def _softmax(x, axis=-1):
    return jax.nn.softmax(x, axis=axis)

def _gelu(x):
    return jax.nn.gelu(x, approximate=True)

def _silu(x):
    return jax.nn.silu(x)

def _sigmoid(x):
    return jax.nn.sigmoid(x)

def _layernorm(x, axis=-1, eps=1e-05):
    m = jnp.mean(x, axis=axis, keepdims=True)
    v = jnp.var(x, axis=axis, keepdims=True)
    return (x - m) / jnp.sqrt(v + eps)

def _scatter_add(tgt, idx, src, axis=0):
    return tgt.at[idx].add(src)

def _segment_sum(src, seg, n):
    return jax.ops.segment_sum(src, seg, n)
kernel_name = 'mk_gnn_preln_d1_gnn_r8_e1dc40'

def setup_inputs(seed: int=0):
    np.random.seed(seed)
    _w = jnp.asarray

    def _rec_inputs():
        import jax
        import jax.numpy as jnp
        _gk = jax.random.key(seed)
        x = -0.000202 + 1 * jax.random.normal(jax.random.fold_in(_gk, 1), (12500, 128), jnp.float32)
        src = jax.random.randint(jax.random.fold_in(_gk, 2), (200000,), 0, 12500, jnp.int32)
        dst = jax.random.randint(jax.random.fold_in(_gk, 3), (200000,), 0, 12500, jnp.int32)
        _o = jnp.argsort(dst, stable=True)
        src = src[_o]
        dst = dst[_o]
        edge_attr_128 = -8.16379e-05 + 0.999858 * jax.random.normal(jax.random.fold_in(_gk, 12), (200000, 128), jnp.float32)
        edge_weight = jax.random.uniform(jax.random.fold_in(_gk, 13), (200000,), jnp.float32, 0.0, 0.999998)
        return (x, src, dst, edge_attr_128, edge_weight)
    x, src, dst, edge_attr_128, edge_weight = _rec_inputs()

    def _L0_gnn_setup():
        import jax, jax.numpy as jnp
        import numpy as np
        N_NODES = 6250
        N_EDGES = 100000
        D = 128
        EPS = 1e-12
        key = jax.random.key(seed)
        ks = jax.random.split(key, 12)
        s = 1.0 / np.sqrt(D)
        return {'node_features': jax.random.normal(ks[0], (N_NODES, D), jnp.float32), 'edge_features': jax.random.normal(ks[1], (N_EDGES, D), jnp.float32), 'src': jax.random.randint(ks[2], (N_EDGES,), 0, N_NODES, jnp.int32), 'dst': jax.random.randint(ks[3], (N_EDGES,), 0, N_NODES, jnp.int32), 'edge_weight_raw': jax.random.uniform(ks[4], (N_EDGES,), jnp.float32), 'W_pool': jax.random.normal(ks[5], (D, D), jnp.float32) * s, 'b_pool': jnp.zeros((D,), jnp.float32), 'W1_self': jax.random.normal(ks[6], (D, D), jnp.float32) * s, 'W1_neigh': jax.random.normal(ks[7], (D, D), jnp.float32) * s, 'b1': jnp.zeros((D,), jnp.float32), 'W2_self': jax.random.normal(ks[8], (D, D), jnp.float32) * s, 'W2_neigh': jax.random.normal(ks[9], (D, D), jnp.float32) * s, 'b2': jnp.zeros((D,), jnp.float32)}
    _L0_gnn_all = _L0_gnn_setup()
    _L0_gnn_in = {k: v for k, v in _L0_gnn_all.items() if k in ('W_pool', 'b_pool', 'W1_self', 'W1_neigh', 'b1', 'W2_self', 'W2_neigh', 'b2')}
    del _L0_gnn_all
    return {'x': x, 'src': src, 'dst': dst, 'edge_attr_128': edge_attr_128, 'edge_weight': edge_weight, 'L0_gnn_W_pool': _L0_gnn_in['W_pool'], 'L0_gnn_b_pool': _L0_gnn_in['b_pool'], 'L0_gnn_W1_self': _L0_gnn_in['W1_self'], 'L0_gnn_W1_neigh': _L0_gnn_in['W1_neigh'], 'L0_gnn_b1': _L0_gnn_in['b1'], 'L0_gnn_W2_self': _L0_gnn_in['W2_self'], 'L0_gnn_W2_neigh': _L0_gnn_in['W2_neigh'], 'L0_gnn_b2': _L0_gnn_in['b2']}

def reference(x, src, dst, edge_attr_128, edge_weight, L0_gnn_W_pool, L0_gnn_b_pool, L0_gnn_W1_self, L0_gnn_W1_neigh, L0_gnn_b1, L0_gnn_W2_self, L0_gnn_W2_neigh, L0_gnn_b2):
    import jax
    import jax.numpy as jnp

    def _L0_gnn_ref(node_features, edge_features, src, dst, edge_weight_raw, W_pool, b_pool, W1_self, W1_neigh, b1, W2_self, W2_neigh, b2):
        import jax, jax.numpy as jnp
        import numpy as np
        N_NODES = 6250
        N_EDGES = 100000
        D = 128
        EPS = 1e-12
        N = node_features.shape[0]
        deg = jax.ops.segment_sum(jnp.ones_like(edge_weight_raw), dst, num_segments=N)
        wsum = jax.ops.segment_sum(edge_weight_raw, dst, num_segments=N)
        w = edge_weight_raw / jnp.maximum(wsum, EPS)[dst]
        feat = jax.nn.relu(node_features @ W_pool + b_pool)
        msg = feat[src] * w[:, None]
        neigh = jax.ops.segment_max(msg, dst, num_segments=N)
        neigh = jnp.where(deg[:, None] > 0, neigh, 0.0)
        rst = node_features @ W1_self + neigh @ W1_neigh + b1
        nrm = jnp.linalg.norm(rst, axis=1, keepdims=True)
        rst = rst / jnp.maximum(nrm, EPS)
        h = jax.nn.relu(rst)
        msg2 = h[src] * w[:, None]
        neigh2 = jax.ops.segment_sum(msg2, dst, num_segments=N) / jnp.maximum(deg, 1.0)[:, None]
        out = jax.nn.relu(h @ W2_self + neigh2 @ W2_neigh + b2)
        return out
    h = jnp.maximum(_layernorm(x, axis=-1), 0.0)
    x = x + _L0_gnn_ref(h, edge_attr_128, src, dst, edge_weight, L0_gnn_W_pool, L0_gnn_b_pool, L0_gnn_W1_self, L0_gnn_W1_neigh, L0_gnn_b1, L0_gnn_W2_self, L0_gnn_W2_neigh, L0_gnn_b2)
    return x

_drawn_inputs = setup_inputs


def setup_inputs(seed=0):
    import zlib

    import numpy as np

    out = dict(_drawn_inputs(seed))
    spreads = {'L0_gnn_b_pool': (0.0, 0.8), 'L0_gnn_b1': (0.0, 0.8), 'L0_gnn_b2': (0.0, 0.1)}
    factors = {'edge_weight': 8.0, 'L0_gnn_W_pool': 8.0, 'L0_gnn_W1_neigh': 8.0, 'L0_gnn_W2_neigh': 8.0}
    for name, (base, spread) in spreads.items():
        noise = np.random.default_rng([zlib.crc32(name.encode()), seed]).standard_normal(out[name].shape)
        drawn = base * np.exp(spread * noise) if base else spread * noise
        out[name] = jnp.asarray(drawn.astype(out[name].dtype))
    for name, factor in factors.items():
        out[name] = (out[name] * factor).astype(out[name].dtype)
    return out
```

```python
from contextlib import ExitStack

import concourse.bass as bass
from concourse import mybir

P = 128
D = 128
N = 12500
E = 200000
NT = 98
NP = NT * P
TS = 1563
EP = TS * P
T = 16
NB = (TS + T - 1) // T
GT = 4
NGR = (NT + GT - 1) // GT
NG = 16
NS = 3
RW = D + 1
NRS = 3
NEG = -1.0e38
TINY = 1e-12

ALU = mybir.AluOpType
ACT = mybir.ActivationFunctionType
F32 = mybir.dt.float32
BF16 = mybir.dt.bfloat16
I32 = mybir.dt.int32


def tiles_of(g):
    return range(g * GT, min(g * GT + GT, NT))


def steps_of(b):
    return range(b * T, min(b * T + T, TS))


def hist_of(b):
    return [k for k in (2 * b, 2 * b + 1) if k < NB]


def build(nc, x, src, dstx, ew, w_pool, b_pool, w1s, w1n, b1, w2s, w2n, b2, out):
    feat = nc.dram_tensor("feat_tab", (NP, D), F32).ap()
    htab = nc.dram_tensor("h_tab", (NP, D), F32).ap()
    scan1 = nc.dram_tensor("scan1", (EP, RW), F32).ap()
    scan2 = nc.dram_tensor("scan2", (EP, D), F32).ap()

    with ExitStack() as ctx:
        def sb(name, shape, dt=F32):
            return ctx.enter_context(nc.sbuf_tensor(name, shape, dt))

        def ps(name, shape, dt=F32):
            return ctx.enter_context(nc.psum_tensor(name, shape, dt))

        def sem(name):
            return ctx.enter_context(nc.semaphore(name))

        A = sb("A", [P, NT, D])
        G = sb("G", [P, NG, D])
        S = sb("S", [P, NS, T, RW])
        HI = sb("HI", [P, 2, T, NT], BF16)
        LO = sb("LO", [P, 2, T, P], BF16)
        SRC = sb("SRC", [P, TS], I32)
        CUR = sb("CUR", [P, TS], I32)
        PRV = sb("PRV", [P, TS], I32)
        EW = sb("EW", [P, TS])
        M = sb("M", [P, TS])
        C = sb("C", [P, TS])
        WS = sb("WS", [P, TS])
        TMP = sb("TMP", [P, TS])
        HB = sb("HB", [P, TS], BF16)
        LB = sb("LB", [P, TS], BF16)
        NR = sb("NR", [P, NRS, GT, RW])
        NTT = sb("NTT", [P, 2, GT, P])
        RST = sb("RST", [P, 3, GT, D])
        X = sb("X", [P, 3, GT, D])
        F = sb("F", [P, 3, GT, D])
        FR = sb("FR", [P, RW])
        CX = sb("CX", [P, P + 1])
        W = sb("W", [P, 5, D])
        BR = sb("BR", [1, 3, D])
        ident = sb("ident", [P, P])
        upper = sb("upper", [P, P])
        ones = sb("ones", [P, P])
        iot = sb("iot", [P, P], I32)
        iob = sb("iob", [P, P], BF16)
        qi = sb("qi", [P, 1], I32)
        qb = sb("qb", [P, 1])
        qf = sb("qf", [P, 1])
        cnt = sb("cnt", [P, 1])
        q = sb("q", [P, 1], I32)
        ac = sb("ac", [P, 1])
        eqf = sb("eqf", [P, 1])
        dg = sb("dg", [P, 2, P])
        abc = sb("abc", [P, P])
        cbc = sb("cbc", [P, P])
        cwx = sb("cwx", [P, P + 1])
        cw1 = sb("cw1", [P, 1])
        scr = sb("scr", [P, P])
        eps5 = sb("eps5", [P, 1])
        st6 = sb("st6", [P, 2, GT, 6])
        mv = sb("mv", [P, NGR * GT, 2])
        sd = sb("sd", [P, NGR * GT])
        rstd = sb("rstd", [P, NGR * GT])
        nmr = sb("nmr", [P, NGR * GT])
        deg = sb("deg", [P, NT])
        tot = sb("tot", [P, NT])
        inc = sb("inc", [P, NT])
        ef = sb("ef", [P, NT])
        eidx = sb("eidx", [P, NT], I32)
        has = sb("has", [P, NT])
        rdeg = sb("rdeg", [P, NT])
        sc1 = sb("sc1", [P, NT])
        sc2 = sb("sc2", [P, NT])
        ss = sb("ss", [P, NT])
        nr = sb("nr", [P, NT])
        rn = sb("rn", [P, NT])

        pT = [ps(f"pT{i}", [P, GT, P]) for i in range(2)]
        pM = [ps(f"pM{i}", [P, GT, D]) for i in range(2)]
        pH = ps("pH", [P, 512])
        pR = [ps(f"pR{i}", [P, 512]) for i in range(2)]
        pC = ps("pC", [P, 512])

        s_w = sem("s_w")
        s_b = sem("s_b")
        s_src = sem("s_src")
        s_dst = sem("s_dst")
        s_ew = sem("s_ew")
        s_cst = sem("s_cst")
        s_x = [sem(f"s_x{i}") for i in range(3)]
        s_var = sem("s_var")
        s_sq = sem("s_sq")
        s_st = sem("s_st")
        s_norm = sem("s_norm")
        s_tp = sem("s_tp")
        s_h0 = sem("s_h0")
        s_pm = sem("s_pm")
        s_feat = sem("s_feat")
        s_fst = [sem(f"s_fst{i}") for i in range(3)]
        s_v = sem("s_v")
        s_dg = sem("s_dg")
        s_bc = sem("s_bc")
        s_q = sem("s_q")
        s_g = [sem(f"s_g{i}") for i in range(NG)]
        s_mul = sem("s_mul")
        s_cmb = sem("s_cmb")
        s_wc = sem("s_wc")
        s_sst = [sem(f"s_sst{i}") for i in range(NS)]
        s_oh = sem("s_oh")
        s_hist = sem("s_hist")
        s_hc = sem("s_hc")
        s_cum = sem("s_cum")
        s_e = sem("s_e")
        s_rp = sem("s_rp")
        s_rc = sem("s_rc")
        s_lt = sem("s_lt")
        s_cx = sem("s_cx")
        s_cp = sem("s_cp")
        s_fg = sem("s_fg")
        s_ff = sem("s_ff")
        s_fs = sem("s_fs")
        s_n = [sem(f"s_n{i}") for i in range(NRS * GT)]
        s_sc = sem("s_sc")
        s_mt = sem("s_mt")
        s_nt = sem("s_nt")
        s_mm = sem("s_mm")
        s_rst = sem("s_rst")
        s_ssq = sem("s_ssq")
        s_nsq = sem("s_nsq")
        s_rn = sem("s_rn")
        s_hn = sem("s_hn")
        s_hst = [sem(f"s_hst{i}") for i in range(3)]
        s_qt = sem("s_qt")
        s_qh = sem("s_qh")
        s_qp = sem("s_qp")
        s_qc = sem("s_qc")
        s_x2 = [sem(f"s_xx{i}") for i in range(3)]
        s_y = sem("s_y")
        s_ost = [sem(f"s_ost{i}") for i in range(3)]

        def rows(tab, g):
            n = len(tiles_of(g))
            return tab[g * GT * P:(g * GT + n) * P, :].rearrange("(j p) d -> p j d", p=P)

        def uses(slot, n, of):
            return len(range(slot, of, n))

        def all_done(eng, sems, of, times=1):
            for i, s in enumerate(sems):
                eng.wait_ge(s, 16 * uses(i, len(sems), of) * times)

        def arrived(eng, sems, i, of=0):
            n = len(sems)
            eng.wait_ge(sems[i % n], 16 * (uses(i % n, n, of) + i // n + 1))

        block = ctx.enter_context(nc.Block())

        @block.sync
        def _(sp):
            def load_x(g, sems):
                sp.dma_start(X[:, g % 3, 0:len(tiles_of(g)), :], rows(x, g)).then_inc(sems[g % 3], 16)

            load_x(0, s_x)
            sp.dma_start(W[:, 0, :], w_pool).then_inc(s_w, 16)
            for i, b in enumerate((b_pool, b1, b2)):
                sp.dma_start(BR[:, i, :], b.rearrange("(a d) -> a d", a=1)).then_inc(s_b, 16)
            load_x(1, s_x)
            load_x(2, s_x)
            sp.dma_start(CUR[:, :], dstx[1:EP + 1].rearrange("(p t) -> p t", p=P)).then_inc(s_dst, 16)
            sp.dma_start(PRV[:, :], dstx[0:EP].rearrange("(p t) -> p t", p=P)).then_inc(s_dst, 16)
            sp.dma_start(SRC[:, :], src.rearrange("(p t) -> p t", p=P)).then_inc(s_src, 16)
            sp.dma_start(EW[:, :], ew.rearrange("(p t) -> p t", p=P)).then_inc(s_ew, 16)
            for i, w in enumerate((w1s, w1n, w2s, w2n)):
                sp.dma_start(W[:, i + 1, :], w).then_inc(s_w, 16)
            for g in range(NGR):
                if g + 3 < NGR:
                    sp.wait_ge(s_tp, g + 1)
                    load_x(g + 3, s_x)
                sp.wait_ge(s_feat, g + 1)
                sp.dma_start(rows(feat, g), F[:, g % 3, 0:len(tiles_of(g)), :]).then_inc(s_fst[g % 3], 16)

            def store_blocks(phase):
                w = RW if phase == 0 else D
                tab = (scan1 if phase == 0 else scan2).rearrange("(p t) d -> p t d", p=P)
                for b in range(NB):
                    r = steps_of(b)
                    sp.wait_ge(s_cmb, phase * TS + r[-1] + 1)
                    if phase == 0:
                        sp.wait_ge(s_wc, b + 1)
                    sp.dma_start(tab[:, r[0]:r[-1] + 1, :], S[:, b % NS, 0:len(r), 0:w])\
                        .then_inc(s_sst[b % NS], 16)

            store_blocks(0)
            for g in range(NGR):
                sp.wait_ge(s_hn, g + 1)
                sp.dma_start(rows(htab, g), A[:, g * GT:g * GT + len(tiles_of(g)), :])\
                    .then_inc(s_hst[g % 3], 16)
            store_blocks(1)
            for g in range(3):
                load_x(g, s_x2)
            for g in range(NGR):
                sp.wait_ge(s_y, g + 1)
                sp.dma_start(rows(out, g), F[:, g % 3, 0:len(tiles_of(g)), :]).then_inc(s_ost[g % 3], 16)
                if g + 3 < NGR:
                    load_x(g + 3, s_x2)
            all_done(sp, s_ost, NGR)

        @block.gpsimd
        def _(pool):
            pool.memset(ident[:, :], 0.0).then_inc(s_cst, 1)
            pool.memset(ones[:, :], 1.0).then_inc(s_cst, 1)
            pool.memset(upper[:, :], 1.0).then_inc(s_cst, 1)
            pool.iota(iot[:, :], pattern=[[1, P]], base=0, channel_multiplier=0).then_inc(s_cst, 1)
            pool.iota(qi[:, :], pattern=[[0, 1]], base=-1, channel_multiplier=TS).then_inc(s_cst, 1)
            pool.wait_ge(s_cst, 5)
            pool.affine_select(out=ident[:, :], in_=ident[:, :], compare_op=ALU.not_equal, fill=1.0,
                               base=0, pattern=[[1, P]], channel_multiplier=-1).then_inc(s_cst, 1)
            pool.affine_select(out=upper[:, :], in_=upper[:, :], compare_op=ALU.is_ge, fill=0.0,
                               base=0, pattern=[[1, P]], channel_multiplier=-1).then_inc(s_cst, 1)

            def gather(dst, table, idx, s):
                pool.indirect_dma_start(out=dst, out_offset=None, in_=table,
                                        in_offset=bass.IndirectOffsetOnAxis(ap=idx, axis=0)).then_inc(s, 16)

            def edge_phase(phase):
                table = (feat, htab)[phase]
                for t in range(TS):
                    if t >= NG or phase:
                        pool.wait_ge(s_cmb, phase * TS + t - NG + 1)
                    gather(G[:, t % NG, :], table, SRC[:, t:t + 1], s_g[t % NG])

            def fix_runs(phase):
                tab = (scan1, scan2)[phase]
                w = (RW, D)[phase]
                all_done(pool, s_sst, NB, phase + 1)
                if phase == 0:
                    pool.wait_ge(s_q, 1)
                gather(FR[:, 0:w], tab, q[:, 0:1], s_fg)
                pool.wait_ge(s_ff, phase + 1)
                pool.indirect_dma_start(out=tab, out_offset=bass.IndirectOffsetOnAxis(ap=q[:, 0:1], axis=0),
                                        in_=FR[:, 0:w], in_offset=None).then_inc(s_fs, 16)
                pool.wait_ge(s_fs, 16 * (phase + 1))

            def node_rows(phase):
                tab = (scan1, scan2)[phase]
                w = (RW, D)[phase]
                if phase == 0:
                    pool.wait_ge(s_e, 1)
                for j in range(NT):
                    g = j // GT
                    if j % GT == 0 and g >= NRS:
                        pool.wait_ge(s_mt, phase * NGR + g - NRS + 1)
                    gather(NR[:, g % NRS, j % GT, 0:w], tab, eidx[:, j:j + 1], s_n[j % (NRS * GT)])

            pool.wait_ge(s_src, 16)
            all_done(pool, s_fst, NGR)
            edge_phase(0)
            fix_runs(0)
            node_rows(0)
            all_done(pool, s_hst, NGR)
            edge_phase(1)
            fix_runs(1)
            node_rows(1)

        @block.scalar
        def _(act):
            act.wait_ge(s_v, 1)
            for i in range(NGR + 3):
                if i < NGR:
                    r = tiles_of(i)
                    act.wait_ge(s_var, i + 1)
                    act.activation(sd[:, r[0]:r[-1] + 1], mv[:, r[0]:r[-1] + 1, 1], ACT.Sqrt,
                                   bias=eps5[:, 0:1]).then_inc(s_sq, 1)
                g = i - 1
                if 0 <= g < NGR:
                    act.wait_ge(s_st, g + 1)
                    for j in tiles_of(g):
                        ins = act.activation(X[:, g % 3, j % GT, :], X[:, g % 3, j % GT, :], ACT.Relu,
                                             scale=rstd[:, j:j + 1], bias=nmr[:, j:j + 1])
                    ins.then_inc(s_norm, 1)
                g = i - 3
                if 0 <= g < NGR:
                    act.wait_ge(s_pm, g + 1)
                    if g >= 3:
                        arrived(act, s_fst, g - 3)
                    n = len(tiles_of(g))
                    act.activation(F[:, g % 3, 0:n, :], pM[g % 2][:, 0:n, :], ACT.Relu).then_inc(s_feat, 1)

            def multiply(phase, t):
                arrived(act, s_g, t, phase * TS)
                act.activation(G[:, t % NG, :], G[:, t % NG, :], ACT.Copy,
                               scale=EW[:, t:t + 1]).then_inc(s_mul, 1)

            act.wait_ge(s_ew, 16)
            for b in range(NB):
                for t in steps_of(b):
                    multiply(0, t)
                act.wait_ge(s_rp, b + 1)
                act.activation(A[:, b, :], pR[b % 2][:, 0:D], ACT.Copy).then_inc(s_rc, 1)

            for i in range(NGR + 1):
                if i < NGR:
                    r = tiles_of(i)
                    act.wait_ge(s_rst, i + 1)
                    for j in r:
                        ins = act.activation(F[:, i % 3, j % GT, :], RST[:, i % 3, j % GT, :], ACT.Square,
                                             accum_out=ss[:, j:j + 1])
                    ins.then_inc(s_ssq, 1)
                    act.wait_ge(s_ssq, i + 1)
                    act.activation(nr[:, r[0]:r[-1] + 1], ss[:, r[0]:r[-1] + 1], ACT.Sqrt).then_inc(s_nsq, 1)
                g = i - 1
                if g >= 0:
                    act.wait_ge(s_rn, g + 1)
                    for j in tiles_of(g):
                        ins = act.activation(A[:, j, :], RST[:, g % 3, j % GT, :], ACT.Relu,
                                             scale=rn[:, j:j + 1])
                    ins.then_inc(s_hn, 1)

            for b in range(NB):
                for t in steps_of(b):
                    multiply(1, t)
                act.wait_ge(s_qt, b + 1)
                act.activation(NTT[:, 0, b % 2, :], pR[0][:, 0:P], ACT.Copy).then_inc(s_qh, 1)
                if b == 0:
                    all_done(act, s_hst, NGR)
                act.wait_ge(s_qp, b + 1)
                act.activation(A[:, b, :], pR[1][:, 0:D], ACT.Copy).then_inc(s_qc, 1)

        @block.vector
        def _(dve):
            chain = [0]

            def link(ins):
                chain[0] += 1
                ins.then_inc(s_v, 1)
                dve.wait_ge(s_v, chain[0])

            link(dve.memset(eps5[:, :], 1e-5))
            for i in range(NGR + 2):
                if i < NGR:
                    r = tiles_of(i)
                    arrived(dve, s_x, i)
                    for j in r:
                        ins = dve.bn_stats(st6[:, i % 2, j % GT, :], X[:, i % 3, j % GT, :])
                    link(ins)
                    for j in r:
                        ins = dve.bn_aggr(mv[:, j, :], st6[:, i % 2, j % GT, :])
                    ins.then_inc(s_var, 1)
                g = i - 1
                if 0 <= g < NGR:
                    r = tiles_of(g)
                    c = slice(r[0], r[-1] + 1)
                    dve.wait_ge(s_sq, g + 1)
                    link(dve.reciprocal(rstd[:, c], sd[:, c]))
                    dve.scalar_tensor_tensor(out=nmr[:, c], in0=mv[:, c, 0], scalar=-1.0, in1=rstd[:, c],
                                             op0=ALU.mult, op1=ALU.mult).then_inc(s_st, 1)
                g = i - 2
                if 0 <= g < NGR:
                    n = len(tiles_of(g))
                    dve.wait_ge(s_tp, g + 1)
                    dve.tensor_copy(A[:, g * GT:g * GT + n, :], pT[g % 2][:, 0:n, :]).then_inc(s_h0, 1)

            dve.wait_ge(s_dst, 32)
            dve.wait_ge(s_ew, 16)
            dve.wait_ge(s_cst, 7)
            link(dve.tensor_tensor(M[:, :], CUR[:, :], PRV[:, :], ALU.is_equal))
            link(dve.tensor_scalar(C[:, :], M[:, :], -NEG, NEG, ALU.mult, ALU.add))
            dve.tensor_copy(TMP[:, :], CUR[:, :])
            link(dve.tensor_copy(qb[:, :], qi[:, :]))
            dve.tensor_tensor(eqf[:, :], TMP[:, 0:1], TMP[:, TS - 1:TS], ALU.is_equal)
            link(dve.tensor_scalar(WS[:, :], TMP[:, :], TMP[:, 0:1], None, ALU.is_equal, ALU.add,
                                   accum_out=cnt[:, :]))
            link(dve.tensor_tensor(ac[:, :], eqf[:, :], M[:, 0:1], ALU.mult))
            dve.tensor_tensor(q[:, :], qb[:, :], cnt[:, :], ALU.add).then_inc(s_q, 1)
            link(dve.tensor_tensor_scan(TMP[:, :], M[:, :], EW[:, :], 0.0, ALU.mult, ALU.add))
            dve.tensor_scalar(dg[:, 0, :], ident[:, :], ac[:, 0:1], None, ALU.mult)
            dve.tensor_scalar(dg[:, 1, :], ident[:, :], TMP[:, TS - 1:TS], None, ALU.mult).then_inc(s_dg, 1)
            dve.memset(CX[:, 0:1], 0.0)
            dve.memset(cwx[:, 0:1], 0.0)
            dve.tensor_scalar(PRV[:, :], CUR[:, :], 7, None, ALU.logical_shift_right)
            link(dve.tensor_copy(iob[:, :], iot[:, :]))
            dve.tensor_copy(HB[:, :], PRV[:, :])
            dve.wait_ge(s_bc, 1)
            link(dve.tensor_copy(abc[:, :], pC[:, 0:P]))
            link(dve.tensor_scalar(cbc[:, :], abc[:, :], -NEG, NEG, ALU.mult, ALU.add))
            link(dve.tensor_tensor_scan(cwx[:, 1:P + 1], abc[:, :], pC[:, P:2 * P], 0.0, ALU.mult, ALU.add))
            link(dve.tensor_tensor(scr[:, :], cwx[:, 0:P], ident[:, :], ALU.mult))
            link(dve.tensor_reduce(cw1[:, :], scr[:, :], mybir.AxisListType.X, ALU.add))
            link(dve.tensor_tensor_scan(WS[:, :], M[:, :], EW[:, :], cw1[:, 0:1], ALU.mult, ALU.add))
            link(dve.tensor_scalar(CUR[:, :], CUR[:, :], 127, None, ALU.bitwise_and))
            link(dve.tensor_copy(LB[:, :], CUR[:, :]))

            def combine(phase, t):
                b, i = t // T, t % T
                g = G[:, t % NG, :]
                o = S[:, b % NS, i, 0:D]
                if i == 0 and b >= NS:
                    arrived(dve, s_sst, b - NS, phase * NB)
                elif i == 0 and phase:
                    dve.wait_ge(s_sst[b], 16 * uses(b, NS, NB))
                dve.wait_ge(s_mul, phase * TS + t + 1)
                if t == 0:
                    dve.tensor_copy(o, g).then_inc(s_cmb, 1)
                    return
                dve.wait_ge(s_cmb, phase * TS + t)
                prev = S[:, (t - 1) // T % NS, (t - 1) % T, 0:D]
                if phase == 0:
                    ins = dve.scalar_tensor_tensor(out=o, in0=prev, scalar=C[:, t:t + 1], in1=g,
                                                   op0=ALU.add, op1=ALU.max)
                else:
                    ins = dve.scalar_tensor_tensor(out=o, in0=prev, scalar=M[:, t:t + 1], in1=g,
                                                   op0=ALU.mult, op1=ALU.add)
                ins.then_inc(s_cmb, 1)

            def one_hots(k):
                r = steps_of(k)
                n = len(r)
                if k >= 2:
                    dve.wait_ge(s_hist, k - 1)
                c = slice(r[0], r[-1] + 1)
                dve.tensor_tensor(HI[:, k % 2, 0:n, :], HB[:, c].unsqueeze(2).to_broadcast([P, n, NT]),
                                  iob[:, 0:NT].unsqueeze(1).to_broadcast([P, n, NT]), ALU.is_equal)
                dve.tensor_tensor(LO[:, k % 2, 0:n, :], LB[:, c].unsqueeze(2).to_broadcast([P, n, P]),
                                  iob[:, :].unsqueeze(1).to_broadcast([P, n, P]),
                                  ALU.is_equal).then_inc(s_oh, 1)

            def run_ends():
                dve.wait_ge(s_hist, NB)
                dve.tensor_copy(deg[:, :], pH[:, 0:NT]).then_inc(s_hc, 1)
                dve.wait_ge(s_hc, 1)
                dve.tensor_scalar(has[:, :], deg[:, :], 1.0, None, ALU.min)
                link(dve.tensor_scalar(ef[:, :], deg[:, :], 1.0, None, ALU.max))
                link(dve.reciprocal(rdeg[:, :], ef[:, :]))
                dve.wait_ge(s_cum, 1)
                link(dve.tensor_copy(tot[:, :], pC[:, 384:384 + NT]))
                link(dve.tensor_tensor_scan(inc[:, :], ones[:, 0:NT], tot[:, :], 0.0, ALU.mult, ALU.add))
                link(dve.scalar_tensor_tensor(out=ef[:, :], in0=inc[:, :], scalar=-1.0, in1=tot[:, :],
                                              op0=ALU.add, op1=ALU.subtract))
                link(dve.tensor_tensor(inc[:, :], ef[:, :], pC[:, 256:256 + NT], ALU.add))
                dve.tensor_scalar(eidx[:, :], inc[:, :], 0.0, None, ALU.max).then_inc(s_e, 1)

            def carry(phase):
                w = (abc, cbc)[phase == 0]
                dve.wait_ge(s_lt, phase + 1)
                dve.tensor_tensor_scan(CX[:, 1:P + 1], w[:, :], pC[:, 0:P], 0.0,
                                       (ALU.mult, ALU.add)[phase == 0],
                                       (ALU.add, ALU.max)[phase == 0]).then_inc(s_cx, 1)
                dve.wait_ge(s_cp, phase + 1)
                link(dve.tensor_scalar(scr[:, :], pC[:, P:2 * P], (M, C)[phase == 0][:, 0:1], None,
                                       (ALU.mult, ALU.add)[phase == 0]))
                dve.wait_ge(s_fg, 16 * (phase + 1))
                dve.tensor_tensor(FR[:, 0:D], FR[:, 0:D], scr[:, :],
                                  (ALU.add, ALU.max)[phase == 0]).then_inc(s_ff, 1)

            for b in range(NB):
                for t in steps_of(b):
                    combine(0, t)
                r = steps_of(b)
                dve.tensor_copy(S[:, b % NS, 0:len(r), D], WS[:, r[0]:r[-1] + 1]).then_inc(s_wc, 1)
                for k in hist_of(b):
                    one_hots(k)
                if b == NB // 2 + 1:
                    run_ends()
            carry(0)
            dve.wait_ge(s_rc, NB)

            def scale_rows(phase, g):
                r = tiles_of(g)
                c = slice(r[0], r[-1] + 1)
                n = len(r)
                for j in r:
                    arrived(dve, s_n, j, phase * NT)
                if phase == 0:
                    link(dve.tensor_scalar(sc2[:, c], NR[:, g % NRS, 0:n, D], TINY, None, ALU.max))
                    link(dve.reciprocal(sc1[:, c], sc2[:, c]))
                    link(dve.tensor_tensor(sc1[:, c], sc1[:, c], has[:, c], ALU.mult))
                    dve.tensor_tensor(sc2[:, c], sc1[:, c], rdeg[:, c], ALU.mult)
                sc = (sc1, sc2)[phase]
                for j in r:
                    ins = dve.tensor_scalar(NR[:, g % NRS, j % GT, 0:D], NR[:, g % NRS, j % GT, 0:D],
                                            sc[:, j:j + 1], None, ALU.mult)
                ins.then_inc(s_sc, 1)

            def copy_rows(phase, g):
                n = len(tiles_of(g))
                k = phase * NGR + g
                dve.wait_ge(s_mt, k + 1)
                if g >= 2:
                    dve.wait_ge(s_mm, k - 1)
                dve.tensor_copy(NTT[:, g % 2, 0:n, :], pT[g % 2][:, 0:n, :]).then_inc(s_nt, 1)

            for i in range(NGR + 3):
                if i < NGR:
                    scale_rows(0, i)
                g = i - 1
                if 0 <= g < NGR:
                    copy_rows(0, g)
                g = i - 2
                if 0 <= g < NGR:
                    n = len(tiles_of(g))
                    dve.wait_ge(s_mm, g + 1)
                    if g >= 3:
                        dve.wait_ge(s_hn, g - 2)
                    dve.tensor_tensor(RST[:, g % 3, 0:n, :], pM[g % 2][:, 0:n, :],
                                      A[:, g * GT:g * GT + n, :], ALU.add).then_inc(s_rst, 1)
                g = i - 3
                if 0 <= g < NGR:
                    r = tiles_of(g)
                    c = slice(r[0], r[-1] + 1)
                    dve.wait_ge(s_nsq, g + 1)
                    link(dve.tensor_scalar(nr[:, c], nr[:, c], TINY, None, ALU.max))
                    dve.reciprocal(rn[:, c], nr[:, c]).then_inc(s_rn, 1)

            for t in range(TS):
                combine(1, t)
            carry(1)
            dve.wait_ge(s_qc, NB)

            for i in range(NGR + 2):
                if i < NGR:
                    scale_rows(1, i)
                g = i - 1
                if 0 <= g < NGR:
                    copy_rows(1, g)
                g = i - 2
                if 0 <= g < NGR:
                    n = len(tiles_of(g))
                    dve.wait_ge(s_mm, NGR + g + 1)
                    link(dve.tensor_tensor(RST[:, g % 3, 0:n, :], pM[g % 2][:, 0:n, :],
                                           A[:, g * GT:g * GT + n, :], ALU.add))
                    arrived(dve, s_x2, g)
                    if g >= 3:
                        arrived(dve, s_ost, g - 3)
                    dve.scalar_tensor_tensor(out=F[:, g % 3, 0:n, :], in0=RST[:, g % 3, 0:n, :], scalar=0.0,
                                             in1=X[:, g % 3, 0:n, :], op0=ALU.max,
                                             op1=ALU.add).then_inc(s_y, 1)

        @block.tensor
        def _(pe):
            def project(o, lhs, w, b):
                ins = pe.matmul(o, lhs, W[:, w, :], start=True, stop=b is None)
                if b is not None:
                    ins = pe.matmul(o, ones[0:1, :], BR[:, b, :], start=False, stop=True)
                return ins

            pe.wait_ge(s_cst, 7)
            pe.wait_ge(s_b, 48)
            pe.wait_ge(s_w, 80)
            for i in range(NGR + 1):
                if i < NGR:
                    pe.wait_ge(s_norm, i + 1)
                    if i >= 2:
                        pe.wait_ge(s_h0, i - 1)
                    for j in tiles_of(i):
                        ins = pe.transpose(pT[i % 2][:, j % GT, :], X[:, i % 3, j % GT, :], ident[:, :])
                    ins.then_inc(s_tp, 1)
                g = i - 1
                if g >= 0:
                    pe.wait_ge(s_h0, g + 1)
                    if g >= 2:
                        pe.wait_ge(s_feat, g - 1)
                    for j in tiles_of(g):
                        ins = project(pM[g % 2][:, j % GT, :], A[:, j, :], 0, 0)
                    ins.then_inc(s_pm, 1)

            pe.wait_ge(s_dg, 1)
            pe.matmul(pC[:, 0:P], ones[:, :], dg[:, 0, :], start=True, stop=True)
            pe.matmul(pC[:, P:2 * P], ones[:, :], dg[:, 1, :], start=True, stop=True).then_inc(s_bc, 1)

            def histogram(k):
                pe.wait_ge(s_oh, k + 1)
                r = steps_of(k)
                for i, t in enumerate(r):
                    ins = pe.matmul(pH[:, 0:NT], LO[:, k % 2, i, :], HI[:, k % 2, i, :],
                                    start=(t == 0), stop=(t == TS - 1))
                ins.then_inc(s_hist, 1)

            for b in range(NB):
                if b >= 2:
                    pe.wait_ge(s_rc, b - 1)
                project(pR[b % 2][:, 0:D], A[:, b, :], 1, 1).then_inc(s_rp, 1)
                for k in hist_of(b):
                    histogram(k)
                if b == NB // 2 + 1:
                    pe.wait_ge(s_hc, 1)
                    pe.matmul(pC[:, 256:256 + NT], upper[:, :], deg[:, :], start=True, stop=True)
                    pe.matmul(pC[:, 384:384 + NT], ones[:, :], deg[:, :], start=True,
                              stop=True).then_inc(s_cum, 1)

            def carry(phase):
                pe.wait_ge(s_cmb, (phase + 1) * TS)
                last = TS - 1
                pe.transpose(pC[:, 0:P], S[:, last // T % NS, last % T, 0:D], ident[:, :]).then_inc(s_lt, 1)
                pe.wait_ge(s_cx, phase + 1)
                pe.transpose(pC[:, P:2 * P], CX[:, 0:P], ident[:, :]).then_inc(s_cp, 1)

            def node_stage(phase, read):
                for i in range(NGR + 1):
                    if i < NGR:
                        k = phase * NGR + i
                        pe.wait_ge(s_sc, k + 1)
                        if k >= 2:
                            pe.wait_ge(s_nt, k - 1)
                        for j in tiles_of(i):
                            ins = pe.transpose(pT[i % 2][:, j % GT, :], NR[:, i % NRS, j % GT, 0:D],
                                               ident[:, :])
                        ins.then_inc(s_mt, 1)
                    g = i - 1
                    if g >= 0:
                        pe.wait_ge(s_nt, phase * NGR + g + 1)
                        if g >= 2:
                            pe.wait_ge(read, g - 1)
                        for j in tiles_of(g):
                            ins = project(pM[g % 2][:, j % GT, :], NTT[:, g % 2, j % GT, :],
                                          (2, 4)[phase], None)
                        ins.then_inc(s_mm, 1)

            carry(0)
            node_stage(0, s_rst)
            pe.wait_ge(s_hn, NGR)
            for b in range(NB):
                pe.wait_ge(s_cmb, TS + steps_of(b)[0])
                if b >= 1:
                    pe.wait_ge(s_qh, b)
                pe.transpose(pR[0][:, 0:P], A[:, b, :], ident[:, :]).then_inc(s_qt, 1)
                pe.wait_ge(s_qh, b + 1)
                if b >= 1:
                    pe.wait_ge(s_qc, b)
                project(pR[1][:, 0:D], NTT[:, 0, b % 2, :], 3, 2).then_inc(s_qp, 1)
            carry(1)
            node_stage(1, s_y)


_NAMES = ["x", "src", "dstx", "ew", "w_pool", "b_pool", "w1s", "w1n", "b1", "w2s", "w2n", "b2"]


def kernel(x, src, dst, edge_attr_128, edge_weight, L0_gnn_W_pool, L0_gnn_b_pool, L0_gnn_W1_self,
           L0_gnn_W1_neigh, L0_gnn_b1, L0_gnn_W2_self, L0_gnn_W2_neigh, L0_gnn_b2):
    import numpy as np
    import concourse.bacc as bacc
    from concourse.bass_utils import run_bass_kernel_spmd

    def filled(a, before, n, value):
        a = np.asarray(a)
        o = np.full((n,) + a.shape[1:], value, a.dtype)
        o[before:before + a.shape[0]] = a
        return o

    dstx = filled(dst, 1, EP + 1, N)
    dstx[0] = -1
    given = [filled(x, 0, NP, 0), filled(src, 0, EP, 0), dstx, filled(edge_weight, 0, EP, 0),
             L0_gnn_W_pool, L0_gnn_b_pool, L0_gnn_W1_self, L0_gnn_W1_neigh, L0_gnn_b1,
             L0_gnn_W2_self, L0_gnn_W2_neigh, L0_gnn_b2]
    nc = bacc.Bacc("TRN2", target_bir_lowering=False, num_devices=1)
    arrays, args = {}, []
    for name, a in zip(_NAMES, given):
        a = np.ascontiguousarray(np.asarray(a))
        arrays[f"in_{name}"] = a
        args.append(nc.dram_tensor(f"in_{name}", a.shape, mybir.dt.from_np(a.dtype), kind="ExternalInput").ap())
    out = nc.dram_tensor("out_0", (NP, D), F32, kind="ExternalOutput").ap()
    build(nc, *args, out)
    r = run_bass_kernel_spmd(nc, [arrays], core_ids=[0])
    return r.results[0]["out_0"][:N]
```

```python
from contextlib import ExitStack

import concourse.bass as bass
from concourse import mybir

P = 128
D = 128
N = 12500
E = 200000
NT = 98
NP = NT * P
TS = 1563
EP = TS * P
T = 16
NB = (TS + T - 1) // T
GT = 4
NGR = (NT + GT - 1) // GT
NG = 16
NS = 3
RW = D + 1
NRS = 3
K = 72
NGX = NGR + K // GT
XAT = {320 + 8 * i: i for i in range(K)}
SEQ = [t for t in range(TS) if t not in XAT]
AT = {t: K + n for n, t in enumerate(SEQ)}
H0 = 30
LOADS = [1, 1, 2, 4, 5, 6, 6]
NEG = -1.0e38
TINY = 1e-12

ALU = mybir.AluOpType
ACT = mybir.ActivationFunctionType
F32 = mybir.dt.float32
BF16 = mybir.dt.bfloat16
I32 = mybir.dt.int32


def tiles_of(g):
    if g >= NGR:
        return range(NGR * GT + (g - NGR) * GT, NGR * GT + (g - NGR + 1) * GT)
    return range(g * GT, min(g * GT + GT, NT))


def steps_of(b):
    return range(b * T, min(b * T + T, TS))


def hist_of(b):
    return [k for k in (2 * (b - H0), 2 * (b - H0) + 1) if 0 <= k < NB]


def build(nc, x, src, dstx, ew, w_pool, b_pool, w1s, w1n, b1, w2s, w2n, b2, out):
    feat = nc.dram_tensor("feat_tab", (NP, D), F32).ap()
    htab = nc.dram_tensor("h_tab", (NP, D), F32).ap()
    scan1 = nc.dram_tensor("scan1", (EP, RW), F32).ap()
    scan2 = nc.dram_tensor("scan2", (EP, D), F32).ap()

    with ExitStack() as ctx:
        def sb(name, shape, dt=F32):
            return ctx.enter_context(nc.sbuf_tensor(name, shape, dt))

        def ps(name, shape, dt=F32):
            return ctx.enter_context(nc.psum_tensor(name, shape, dt))

        def sem(name):
            return ctx.enter_context(nc.semaphore(name))

        A = sb("A", [P, NT, D])
        G = sb("G", [P, NG, D])
        S = sb("S", [P, NS, T, RW])
        HI = sb("HI", [P, 2, T, NT], BF16)
        LB32 = sb("LB32", [P, T * P])
        LO = LB32[:, :].bitcast(BF16).rearrange("p (k t n) -> p k t n", k=2, t=T)
        TMP = LB32[:, 0:TS]
        SRC = sb("SRC", [P, TS], I32)
        CUR = sb("CUR", [P, TS], I32)
        PRV = sb("PRV", [P, TS], I32)
        EW = sb("EW", [P, TS])
        M = sb("M", [P, TS])
        C = sb("C", [P, TS])
        WS = sb("WS", [P, TS])
        HB = sb("HB", [P, TS], BF16)
        LB = sb("LB", [P, TS], BF16)
        U = sb("U", [P, K * D])
        XR = U[:, :].rearrange("p (k d) -> p k d", d=D)
        at = [0]

        def part(*shape):
            n = 1
            for k in shape:
                n *= k
            at[0] += n
            assert at[0] <= K * D
            v = U[:, at[0] - n:at[0]]
            return v.rearrange("p (a b c) -> p a b c", b=shape[1], c=shape[2])

        NR = part(NRS, GT, RW)
        NTT = part(2, GT, P)
        RST = part(3, GT, D)
        X = part(3, GT, D)
        BB = sb("BB", [P, D])
        F = sb("F", [P, 3, GT, D])
        FR = sb("FR", [P, RW])
        CX = sb("CX", [P, P + 1])
        W = sb("W", [P, 5, D])
        BR = sb("BR", [1, 2, D])
        ident = sb("ident", [P, P])
        upper = sb("upper", [P, P])
        ones = sb("ones", [P, P])
        iot = sb("iot", [P, P], I32)
        iob = sb("iob", [P, P], BF16)
        qi = sb("qi", [P, 1], I32)
        qb = sb("qb", [P, 1])
        qf = sb("qf", [P, 1])
        cnt = sb("cnt", [P, 1])
        q = sb("q", [P, 1], I32)
        ac = sb("ac", [P, 1])
        eqf = sb("eqf", [P, 1])
        dg = sb("dg", [P, 2, P])
        abc = sb("abc", [P, P])
        cbc = sb("cbc", [P, P])
        cwx = sb("cwx", [P, P + 1])
        cw1 = sb("cw1", [P, 1])
        scr = sb("scr", [P, P])
        eps5 = sb("eps5", [P, 1])
        st6 = sb("st6", [P, 2, GT, 6])
        mv = sb("mv", [P, NGX * GT, 2])
        sd = sb("sd", [P, NGX * GT])
        rstd = sb("rstd", [P, NGX * GT])
        nmr = sb("nmr", [P, NGX * GT])
        deg = sb("deg", [P, NT])
        tot = sb("tot", [P, NT])
        inc = sb("inc", [P, NT])
        ef = sb("ef", [P, NT])
        eidx = sb("eidx", [P, NT], I32)
        has = sb("has", [P, NT])
        rdeg = sb("rdeg", [P, NT])
        sc1 = sb("sc1", [P, NT])
        sc2 = sb("sc2", [P, NT])
        ss = sb("ss", [P, NT])
        nr = sb("nr", [P, NT])
        rn = sb("rn", [P, NT])

        pT = [ps(f"pT{i}", [P, GT, P]) for i in range(2)]
        pM = [ps(f"pM{i}", [P, GT, D]) for i in range(2)]
        pH = ps("pH", [P, 512])
        pR = [ps(f"pR{i}", [P, 512]) for i in range(2)]
        pC = ps("pC", [P, 512])

        s_w = sem("s_w")
        s_b = sem("s_b")
        s_bb = sem("s_bb")
        s_src = sem("s_src")
        s_dst = sem("s_dst")
        s_ew = sem("s_ew")
        s_cst = sem("s_cst")
        s_x = [sem(f"s_x{i}") for i in range(len(LOADS))]
        s_add = sem("s_add")
        s_var = sem("s_var")
        s_sq = sem("s_sq")
        s_st = sem("s_st")
        s_norm = sem("s_norm")
        s_tp = sem("s_tp")
        s_h0 = sem("s_h0")
        s_pm = sem("s_pm")
        s_feat = sem("s_feat")
        s_fst = [sem(f"s_fst{i}") for i in range(3)]
        s_v = sem("s_v")
        s_dg = sem("s_dg")
        s_bc = sem("s_bc")
        s_q = sem("s_q")
        s_g = [sem(f"s_g{i}") for i in range(NG)]
        s_mul = sem("s_mul")
        s_cmb = sem("s_cmb")
        s_wc = sem("s_wc")
        s_sst = [sem(f"s_sst{i}") for i in range(NS)]
        s_oh = sem("s_oh")
        s_hist = sem("s_hist")
        s_hc = sem("s_hc")
        s_cum = sem("s_cum")
        s_e = sem("s_e")
        s_rp = sem("s_rp")
        s_rc = sem("s_rc")
        s_lt = sem("s_lt")
        s_cx = sem("s_cx")
        s_cp = sem("s_cp")
        s_fg = sem("s_fg")
        s_ff = sem("s_ff")
        s_fs = sem("s_fs")
        s_n = [sem(f"s_n{i}") for i in range(NRS * GT)]
        s_sc = sem("s_sc")
        s_mt = sem("s_mt")
        s_nt = sem("s_nt")
        s_mm = sem("s_mm")
        s_rst = sem("s_rst")
        s_ssq = sem("s_ssq")
        s_nsq = sem("s_nsq")
        s_rn = sem("s_rn")
        s_hn = sem("s_hn")
        s_hst = [sem(f"s_hst{i}") for i in range(3)]
        s_qt = sem("s_qt")
        s_qh = sem("s_qh")
        s_qp = sem("s_qp")
        s_qc = sem("s_qc")
        s_x2 = [sem(f"s_xx{i}") for i in range(3)]
        s_y = sem("s_y")
        s_ost = [sem(f"s_ost{i}") for i in range(3)]

        def rows(tab, g):
            n = len(tiles_of(g))
            return tab[g * GT * P:(g * GT + n) * P, :].rearrange("(j p) d -> p j d", p=P)

        def uses(slot, n, of):
            return len(range(slot, of, n))

        def all_done(eng, sems, of, times=1):
            for i, s in enumerate(sems):
                eng.wait_ge(s, 16 * uses(i, len(sems), of) * times)

        def arrived(eng, sems, i, of=0):
            n = len(sems)
            eng.wait_ge(sems[i % n], 16 * (uses(i % n, n, of) + i // n + 1))

        def raw(g):
            if g >= NGR:
                return XR[:, (g - NGR) * GT:(g - NGR + 1) * GT, :]
            return A[:, g * GT:g * GT + len(tiles_of(g)), :]

        def turned(g):
            return F[:, g % 3, :, :] if g >= NGR else raw(g)

        def projected(g):
            return raw(g) if g >= NGR else F[:, g % 3, 0:len(tiles_of(g)), :]

        def raw_arrived(eng, g):
            if g >= NGR:
                for i in range((g - NGR) * GT, (g - NGR + 1) * GT):
                    arrived(eng, s_g, i)
            else:
                eng.wait_ge(s_x[max(i for i in range(len(LOADS)) if sum(LOADS[:i]) <= g)], 16)

        block = ctx.enter_context(nc.Block())

        @block.sync
        def _(sp):
            def load_x(g):
                sp.dma_start(X[:, g % 3, 0:len(tiles_of(g)), :], rows(x, g)).then_inc(s_x2[g % 3], 16)

            sp.dma_start(SRC[:, :], src.rearrange("(p t) -> p t", p=P)).then_inc(s_src, 16)
            g = 0
            for i, n in enumerate(LOADS):
                a, c = g * GT, min((g + n) * GT, NT)
                sp.dma_start(A[:, a:c, :], x[a * P:c * P, :].rearrange("(j p) d -> p j d", p=P)).then_inc(s_x[i], 16)
                g += n
                if i == 1:
                    sp.dma_start(W[:, 0, :], w_pool).then_inc(s_w, 16)
                    sp.dma_start(BB[:, :], b_pool.rearrange("(a d) -> a d", a=1).to_broadcast([P, D])).then_inc(s_bb, 16)
                if i == 3:
                    sp.dma_start(CUR[:, :], dstx[1:EP + 1].rearrange("(p t) -> p t", p=P)).then_inc(s_dst, 16)
                    sp.dma_start(PRV[:, :], dstx[0:EP].rearrange("(p t) -> p t", p=P)).then_inc(s_dst, 16)
                    sp.dma_start(EW[:, :], ew.rearrange("(p t) -> p t", p=P)).then_inc(s_ew, 16)
            for i, b in enumerate((b1, b2)):
                sp.dma_start(BR[:, i, :], b.rearrange("(a d) -> a d", a=1)).then_inc(s_b, 16)
            for i, w in enumerate((w1s, w1n, w2s, w2n)):
                sp.dma_start(W[:, i + 1, :], w).then_inc(s_b, 16)
            for g in range(NGR):
                sp.wait_ge(s_feat, g + 1)
                sp.dma_start(rows(feat, g), F[:, g % 3, 0:len(tiles_of(g)), :]).then_inc(s_fst[g % 3], 16)

            def store_blocks(phase):
                w = RW if phase == 0 else D
                tab = (scan1 if phase == 0 else scan2).rearrange("(p t) d -> p t d", p=P)
                for b in range(NB):
                    r = steps_of(b)
                    sp.wait_ge(s_cmb, phase * TS + r[-1] + 1)
                    if phase == 0:
                        sp.wait_ge(s_wc, b + 1)
                    sp.dma_start(tab[:, r[0]:r[-1] + 1, :], S[:, b % NS, 0:len(r), 0:w])\
                        .then_inc(s_sst[b % NS], 16)

            store_blocks(0)
            for g in range(NGR):
                sp.wait_ge(s_hn, g + 1)
                sp.dma_start(rows(htab, g), A[:, g * GT:g * GT + len(tiles_of(g)), :])\
                    .then_inc(s_hst[g % 3], 16)
            store_blocks(1)
            for g in range(3):
                load_x(g)
            for g in range(NGR):
                sp.wait_ge(s_y, g + 1)
                sp.dma_start(rows(out, g), F[:, g % 3, 0:len(tiles_of(g)), :]).then_inc(s_ost[g % 3], 16)
                if g + 3 < NGR:
                    load_x(g + 3)
            all_done(sp, s_ost, NGR)

        @block.gpsimd
        def _(pool):
            pool.memset(ident[:, :], 0.0).then_inc(s_cst, 1)
            pool.memset(ones[:, :], 1.0).then_inc(s_cst, 1)
            pool.memset(upper[:, :], 1.0).then_inc(s_cst, 1)
            pool.iota(iot[:, :], pattern=[[1, P]], base=0, channel_multiplier=0).then_inc(s_cst, 1)
            pool.iota(qi[:, :], pattern=[[0, 1]], base=-1, channel_multiplier=TS).then_inc(s_cst, 1)
            pool.wait_ge(s_cst, 5)
            pool.affine_select(out=ident[:, :], in_=ident[:, :], compare_op=ALU.not_equal, fill=1.0,
                               base=0, pattern=[[1, P]], channel_multiplier=-1).then_inc(s_cst, 1)
            pool.affine_select(out=upper[:, :], in_=upper[:, :], compare_op=ALU.is_ge, fill=0.0,
                               base=0, pattern=[[1, P]], channel_multiplier=-1).then_inc(s_cst, 1)

            def gather(dst, table, idx, s):
                pool.indirect_dma_start(out=dst, out_offset=None, in_=table,
                                        in_offset=bass.IndirectOffsetOnAxis(ap=idx, axis=0)).then_inc(s, 16)

            def edge_phase(phase):
                table = (feat, htab)[phase]
                for t in range(TS) if phase else SEQ:
                    n = TS + t if phase else AT[t]
                    if phase:
                        pool.wait_ge(s_cmb, TS + t - NG + 1)
                    elif n - NG >= K:
                        pool.wait_ge(s_cmb, SEQ[n - NG - K] + 1)
                    else:
                        pool.wait_ge(s_g[n % NG], 16 * (n // NG))
                    gather(G[:, n % NG, :], table, SRC[:, t:t + 1], s_g[n % NG])

            def fix_runs(phase):
                tab = (scan1, scan2)[phase]
                w = (RW, D)[phase]
                all_done(pool, s_sst, NB, phase + 1)
                if phase == 0:
                    pool.wait_ge(s_q, 1)
                gather(FR[:, 0:w], tab, q[:, 0:1], s_fg)
                pool.wait_ge(s_ff, phase + 1)
                pool.indirect_dma_start(out=tab, out_offset=bass.IndirectOffsetOnAxis(ap=q[:, 0:1], axis=0),
                                        in_=FR[:, 0:w], in_offset=None).then_inc(s_fs, 16)
                pool.wait_ge(s_fs, 16 * (phase + 1))

            def node_rows(phase):
                tab = (scan1, scan2)[phase]
                w = (RW, D)[phase]
                if phase == 0:
                    pool.wait_ge(s_e, 1)
                for j in range(NT):
                    g = j // GT
                    if j % GT == 0 and g >= NRS:
                        pool.wait_ge(s_mt, phase * NGR + g - NRS + 1)
                    gather(NR[:, g % NRS, j % GT, 0:w], tab, eidx[:, j:j + 1], s_n[j % (NRS * GT)])

            pool.wait_ge(s_src, 16)
            for t, i in XAT.items():
                if i >= NG:
                    pool.wait_ge(s_g[i % NG], 16 * (i // NG))
                gather(XR[:, i, :], x, SRC[:, t:t + 1], s_g[i % NG])
            all_done(pool, s_fst, NGR)
            edge_phase(0)
            fix_runs(0)
            node_rows(0)
            all_done(pool, s_hst, NGR)
            edge_phase(1)
            fix_runs(1)
            node_rows(1)

        @block.scalar
        def _(act):
            def deviation(g):
                r = tiles_of(g)
                act.wait_ge(s_var, g + 1)
                act.activation(sd[:, r[0]:r[-1] + 1], mv[:, r[0]:r[-1] + 1, 1], ACT.Sqrt,
                               bias=eps5[:, 0:1]).then_inc(s_sq, 1)

            def normalise(g):
                act.wait_ge(s_st, g + 1)
                for j in tiles_of(g):
                    v = raw(g)[:, j % GT, :]
                    ins = act.activation(v, v, ACT.Relu, scale=rstd[:, j:j + 1], bias=nmr[:, j:j + 1])
                ins.then_inc(s_norm, 1)

            def rectify(g):
                act.wait_ge(s_add, g + 1)
                act.activation(projected(g), projected(g), ACT.Relu).then_inc(s_feat, 1)

            act.wait_ge(s_v, 1)
            for i in range(NGR + 3):
                if i < NGR:
                    deviation(i)
                if 0 <= i - 1 < NGR:
                    normalise(i - 1)
                if 0 <= i - 3 < NGR:
                    rectify(i - 3)

            def multiply(phase, t):
                n = TS + t if phase else AT.get(t)
                if n is None:
                    act.wait_ge(s_feat, NGR + XAT[t] // GT + 1)
                    v = XR[:, XAT[t], :]
                else:
                    arrived(act, s_g, n)
                    v = G[:, n % NG, :]
                act.activation(v, v, ACT.Copy, scale=EW[:, t:t + 1]).then_inc(s_mul, 1)

            act.wait_ge(s_ew, 16)
            for b in range(NB):
                for t in steps_of(b):
                    multiply(0, t)
                act.wait_ge(s_rp, b + 1)
                act.activation(A[:, b, :], pR[b % 2][:, 0:D], ACT.Copy).then_inc(s_rc, 1)
                if b < NGX - NGR:
                    deviation(NGR + b)
                if 0 <= b - 1 < NGX - NGR:
                    normalise(NGR + b - 1)
                if 0 <= b - 3 < NGX - NGR:
                    rectify(NGR + b - 3)

            for i in range(NGR + 1):
                if i < NGR:
                    r = tiles_of(i)
                    act.wait_ge(s_rst, i + 1)
                    for j in r:
                        ins = act.activation(F[:, i % 3, j % GT, :], RST[:, i % 3, j % GT, :], ACT.Square,
                                             accum_out=ss[:, j:j + 1])
                    ins.then_inc(s_ssq, 1)
                    act.wait_ge(s_ssq, i + 1)
                    act.activation(nr[:, r[0]:r[-1] + 1], ss[:, r[0]:r[-1] + 1], ACT.Sqrt).then_inc(s_nsq, 1)
                g = i - 1
                if g >= 0:
                    act.wait_ge(s_rn, g + 1)
                    for j in tiles_of(g):
                        ins = act.activation(A[:, j, :], RST[:, g % 3, j % GT, :], ACT.Relu,
                                             scale=rn[:, j:j + 1])
                    ins.then_inc(s_hn, 1)

            for b in range(NB):
                for t in steps_of(b):
                    multiply(1, t)
                act.wait_ge(s_qt, b + 1)
                act.activation(NTT[:, 0, b % 2, :], pR[0][:, 0:P], ACT.Copy).then_inc(s_qh, 1)
                if b == 0:
                    all_done(act, s_hst, NGR)
                act.wait_ge(s_qp, b + 1)
                act.activation(A[:, b, :], pR[1][:, 0:D], ACT.Copy).then_inc(s_qc, 1)

        @block.vector
        def _(dve):
            chain = [0]

            def link(ins):
                chain[0] += 1
                ins.then_inc(s_v, 1)
                dve.wait_ge(s_v, chain[0])

            link(dve.memset(eps5[:, :], 1e-5))
            def stats(g):
                raw_arrived(dve, g)
                for j in tiles_of(g):
                    ins = dve.bn_stats(st6[:, g % 2, j % GT, :], raw(g)[:, j % GT, :])
                link(ins)
                for j in tiles_of(g):
                    ins = dve.bn_aggr(mv[:, j, :], st6[:, g % 2, j % GT, :])
                ins.then_inc(s_var, 1)

            def scales(g):
                r = tiles_of(g)
                c = slice(r[0], r[-1] + 1)
                dve.wait_ge(s_sq, g + 1)
                link(dve.reciprocal(rstd[:, c], sd[:, c]))
                dve.scalar_tensor_tensor(out=nmr[:, c], in0=mv[:, c, 0], scalar=-1.0, in1=rstd[:, c],
                                         op0=ALU.mult, op1=ALU.mult).then_inc(s_st, 1)

            def turn(g):
                dve.wait_ge(s_tp, g + 1)
                if g == NGR:
                    all_done(dve, s_fst, NGR)
                if g >= NGR + 3:
                    dve.wait_ge(s_pm, g - 2)
                dve.tensor_copy(turned(g), pT[g % 2][:, 0:len(tiles_of(g)), :]).then_inc(s_h0, 1)

            def add_bias(g):
                dve.wait_ge(s_pm, g + 1)
                if 3 <= g < NGR:
                    arrived(dve, s_fst, g - 3)
                n = len(tiles_of(g))
                dve.tensor_tensor(projected(g), pM[g % 2][:, 0:n, :],
                                  BB[:, :].unsqueeze(1).to_broadcast([P, n, D]), ALU.add).then_inc(s_add, 1)

            dve.wait_ge(s_bb, 16)
            for i in range(NGR + 3):
                if i < NGR:
                    stats(i)
                if 0 <= i - 1 < NGR:
                    scales(i - 1)
                if 0 <= i - 2 < NGR:
                    turn(i - 2)
                if 0 <= i - 3 < NGR:
                    add_bias(i - 3)
                if i == 12:
                    dve.wait_ge(s_dst, 32)
                    link(dve.tensor_tensor(M[:, :], CUR[:, :], PRV[:, :], ALU.is_equal))
                    link(dve.tensor_scalar(C[:, :], M[:, :], -NEG, NEG, ALU.mult, ALU.add))

            dve.wait_ge(s_ew, 16)
            dve.wait_ge(s_cst, 7)

            def prelude():
                dve.tensor_copy(TMP[:, :], CUR[:, :])
                link(dve.tensor_copy(qb[:, :], qi[:, :]))
                dve.tensor_tensor(eqf[:, :], TMP[:, 0:1], TMP[:, TS - 1:TS], ALU.is_equal)
                link(dve.tensor_scalar(WS[:, :], TMP[:, :], TMP[:, 0:1], None, ALU.is_equal, ALU.add,
                                       accum_out=cnt[:, :]))
                link(dve.tensor_tensor(ac[:, :], eqf[:, :], M[:, 0:1], ALU.mult))
                dve.tensor_tensor(q[:, :], qb[:, :], cnt[:, :], ALU.add).then_inc(s_q, 1)
                link(dve.tensor_tensor_scan(TMP[:, :], M[:, :], EW[:, :], 0.0, ALU.mult, ALU.add))
                dve.tensor_scalar(dg[:, 0, :], ident[:, :], ac[:, 0:1], None, ALU.mult)
                dve.tensor_scalar(dg[:, 1, :], ident[:, :], TMP[:, TS - 1:TS], None, ALU.mult).then_inc(s_dg, 1)
                dve.memset(CX[:, 0:1], 0.0)
                dve.memset(cwx[:, 0:1], 0.0)
                dve.tensor_scalar(PRV[:, :], CUR[:, :], 7, None, ALU.logical_shift_right)
                link(dve.tensor_copy(iob[:, :], iot[:, :]))
                dve.tensor_copy(HB[:, :], PRV[:, :])
                dve.wait_ge(s_bc, 1)
                link(dve.tensor_copy(abc[:, :], pC[:, 0:P]))
                link(dve.tensor_scalar(cbc[:, :], abc[:, :], -NEG, NEG, ALU.mult, ALU.add))
                link(dve.tensor_tensor_scan(cwx[:, 1:P + 1], abc[:, :], pC[:, P:2 * P], 0.0, ALU.mult, ALU.add))
                link(dve.tensor_tensor(scr[:, :], cwx[:, 0:P], ident[:, :], ALU.mult))
                link(dve.tensor_reduce(cw1[:, :], scr[:, :], mybir.AxisListType.X, ALU.add))
                link(dve.tensor_tensor_scan(WS[:, :], M[:, :], EW[:, :], cw1[:, 0:1], ALU.mult, ALU.add))
                link(dve.tensor_scalar(CUR[:, :], CUR[:, :], 127, None, ALU.bitwise_and))
                link(dve.tensor_copy(LB[:, :], CUR[:, :]))

            def combine(phase, t):
                b, i = t // T, t % T
                n = TS + t if phase else AT.get(t)
                g = XR[:, XAT[t], :] if n is None else G[:, n % NG, :]
                o = S[:, b % NS, i, 0:D]
                if i == 0 and b >= NS:
                    arrived(dve, s_sst, b - NS, phase * NB)
                elif i == 0 and phase:
                    dve.wait_ge(s_sst[b], 16 * uses(b, NS, NB))
                dve.wait_ge(s_mul, phase * TS + t + 1)
                if t == 0:
                    dve.tensor_copy(o, g).then_inc(s_cmb, 1)
                    return
                dve.wait_ge(s_cmb, phase * TS + t)
                prev = S[:, (t - 1) // T % NS, (t - 1) % T, 0:D]
                if phase == 0:
                    ins = dve.scalar_tensor_tensor(out=o, in0=prev, scalar=C[:, t:t + 1], in1=g,
                                                   op0=ALU.add, op1=ALU.max)
                else:
                    ins = dve.scalar_tensor_tensor(out=o, in0=prev, scalar=M[:, t:t + 1], in1=g,
                                                   op0=ALU.mult, op1=ALU.add)
                ins.then_inc(s_cmb, 1)

            def one_hots(k):
                r = steps_of(k)
                n = len(r)
                if k >= 2:
                    dve.wait_ge(s_hist, k - 1)
                c = slice(r[0], r[-1] + 1)
                dve.tensor_tensor(HI[:, k % 2, 0:n, :], HB[:, c].unsqueeze(2).to_broadcast([P, n, NT]),
                                  iob[:, 0:NT].unsqueeze(1).to_broadcast([P, n, NT]), ALU.is_equal)
                dve.tensor_tensor(LO[:, k % 2, 0:n, :], LB[:, c].unsqueeze(2).to_broadcast([P, n, P]),
                                  iob[:, :].unsqueeze(1).to_broadcast([P, n, P]),
                                  ALU.is_equal).then_inc(s_oh, 1)

            def run_ends():
                dve.wait_ge(s_hist, NB)
                dve.tensor_copy(deg[:, :], pH[:, 0:NT]).then_inc(s_hc, 1)
                dve.wait_ge(s_hc, 1)
                dve.tensor_scalar(has[:, :], deg[:, :], 1.0, None, ALU.min)
                link(dve.tensor_scalar(ef[:, :], deg[:, :], 1.0, None, ALU.max))
                link(dve.reciprocal(rdeg[:, :], ef[:, :]))
                dve.wait_ge(s_cum, 1)
                link(dve.tensor_copy(tot[:, :], pC[:, 384:384 + NT]))
                link(dve.tensor_tensor_scan(inc[:, :], ones[:, 0:NT], tot[:, :], 0.0, ALU.mult, ALU.add))
                link(dve.scalar_tensor_tensor(out=ef[:, :], in0=inc[:, :], scalar=-1.0, in1=tot[:, :],
                                              op0=ALU.add, op1=ALU.subtract))
                link(dve.tensor_tensor(inc[:, :], ef[:, :], pC[:, 256:256 + NT], ALU.add))
                dve.tensor_scalar(eidx[:, :], inc[:, :], 0.0, None, ALU.max).then_inc(s_e, 1)

            def carry(phase):
                w = (abc, cbc)[phase == 0]
                dve.wait_ge(s_lt, phase + 1)
                dve.tensor_tensor_scan(CX[:, 1:P + 1], w[:, :], pC[:, 0:P], 0.0,
                                       (ALU.mult, ALU.add)[phase == 0],
                                       (ALU.add, ALU.max)[phase == 0]).then_inc(s_cx, 1)
                dve.wait_ge(s_cp, phase + 1)
                link(dve.tensor_scalar(scr[:, :], pC[:, P:2 * P], (M, C)[phase == 0][:, 0:1], None,
                                       (ALU.mult, ALU.add)[phase == 0]))
                dve.wait_ge(s_fg, 16 * (phase + 1))
                dve.tensor_tensor(FR[:, 0:D], FR[:, 0:D], scr[:, :],
                                  (ALU.add, ALU.max)[phase == 0]).then_inc(s_ff, 1)

            for b in range(NB):
                for t in steps_of(b):
                    combine(0, t)
                if b == 0:
                    prelude()
                r = steps_of(b)
                dve.tensor_copy(S[:, b % NS, 0:len(r), D], WS[:, r[0]:r[-1] + 1]).then_inc(s_wc, 1)
                for k in hist_of(b):
                    one_hots(k)
                if b == H0 + NB // 2 + 1:
                    run_ends()
                if b < NGX - NGR:
                    stats(NGR + b)
                if 0 <= b - 1 < NGX - NGR:
                    scales(NGR + b - 1)
                if 0 <= b - 2 < NGX - NGR:
                    turn(NGR + b - 2)
                if 0 <= b - 3 < NGX - NGR:
                    add_bias(NGR + b - 3)
            carry(0)
            dve.wait_ge(s_rc, NB)

            def scale_rows(phase, g):
                r = tiles_of(g)
                c = slice(r[0], r[-1] + 1)
                n = len(r)
                for j in r:
                    arrived(dve, s_n, j, phase * NT)
                if phase == 0:
                    link(dve.tensor_scalar(sc2[:, c], NR[:, g % NRS, 0:n, D], TINY, None, ALU.max))
                    link(dve.reciprocal(sc1[:, c], sc2[:, c]))
                    link(dve.tensor_tensor(sc1[:, c], sc1[:, c], has[:, c], ALU.mult))
                    dve.tensor_tensor(sc2[:, c], sc1[:, c], rdeg[:, c], ALU.mult)
                sc = (sc1, sc2)[phase]
                for j in r:
                    ins = dve.tensor_scalar(NR[:, g % NRS, j % GT, 0:D], NR[:, g % NRS, j % GT, 0:D],
                                            sc[:, j:j + 1], None, ALU.mult)
                ins.then_inc(s_sc, 1)

            def copy_rows(phase, g):
                n = len(tiles_of(g))
                k = phase * NGR + g
                dve.wait_ge(s_mt, k + 1)
                if g >= 2:
                    dve.wait_ge(s_mm, k - 1)
                dve.tensor_copy(NTT[:, g % 2, 0:n, :], pT[g % 2][:, 0:n, :]).then_inc(s_nt, 1)

            for i in range(NGR + 3):
                if i < NGR:
                    scale_rows(0, i)
                g = i - 1
                if 0 <= g < NGR:
                    copy_rows(0, g)
                g = i - 2
                if 0 <= g < NGR:
                    n = len(tiles_of(g))
                    dve.wait_ge(s_mm, g + 1)
                    if g >= 3:
                        dve.wait_ge(s_hn, g - 2)
                    dve.tensor_tensor(RST[:, g % 3, 0:n, :], pM[g % 2][:, 0:n, :],
                                      A[:, g * GT:g * GT + n, :], ALU.add).then_inc(s_rst, 1)
                g = i - 3
                if 0 <= g < NGR:
                    r = tiles_of(g)
                    c = slice(r[0], r[-1] + 1)
                    dve.wait_ge(s_nsq, g + 1)
                    link(dve.tensor_scalar(nr[:, c], nr[:, c], TINY, None, ALU.max))
                    dve.reciprocal(rn[:, c], nr[:, c]).then_inc(s_rn, 1)

            for t in range(TS):
                combine(1, t)
            carry(1)
            dve.wait_ge(s_qc, NB)

            for i in range(NGR + 2):
                if i < NGR:
                    scale_rows(1, i)
                g = i - 1
                if 0 <= g < NGR:
                    copy_rows(1, g)
                g = i - 2
                if 0 <= g < NGR:
                    n = len(tiles_of(g))
                    dve.wait_ge(s_mm, NGR + g + 1)
                    link(dve.tensor_tensor(RST[:, g % 3, 0:n, :], pM[g % 2][:, 0:n, :],
                                           A[:, g * GT:g * GT + n, :], ALU.add))
                    arrived(dve, s_x2, g)
                    if g >= 3:
                        arrived(dve, s_ost, g - 3)
                    dve.scalar_tensor_tensor(out=F[:, g % 3, 0:n, :], in0=RST[:, g % 3, 0:n, :], scalar=0.0,
                                             in1=X[:, g % 3, 0:n, :], op0=ALU.max,
                                             op1=ALU.add).then_inc(s_y, 1)

        @block.tensor
        def _(pe):
            def project(o, lhs, w, b):
                ins = pe.matmul(o, lhs, W[:, w, :], start=True, stop=b is None)
                if b is not None:
                    ins = pe.matmul(o, ones[0:1, :], BR[:, b, :], start=False, stop=True)
                return ins

            def turn(g):
                pe.wait_ge(s_norm, g + 1)
                if g >= 2:
                    pe.wait_ge(s_h0, g - 1)
                for j in tiles_of(g):
                    ins = pe.transpose(pT[g % 2][:, j % GT, :], raw(g)[:, j % GT, :], ident[:, :])
                ins.then_inc(s_tp, 1)

            def pool_features(g):
                pe.wait_ge(s_h0, g + 1)
                if g >= 2:
                    pe.wait_ge(s_add, g - 1)
                for j in tiles_of(g):
                    ins = project(pM[g % 2][:, j % GT, :], turned(g)[:, j % GT, :], 0, None)
                ins.then_inc(s_pm, 1)

            pe.wait_ge(s_cst, 7)
            pe.wait_ge(s_w, 16)
            for i in range(NGR + 1):
                if i < NGR:
                    turn(i)
                if i >= 1:
                    pool_features(i - 1)
            pe.wait_ge(s_b, 96)

            def histogram(k):
                pe.wait_ge(s_oh, k + 1)
                r = steps_of(k)
                for i, t in enumerate(r):
                    ins = pe.matmul(pH[:, 0:NT], LO[:, k % 2, i, :], HI[:, k % 2, i, :],
                                    start=(t == 0), stop=(t == TS - 1))
                ins.then_inc(s_hist, 1)

            for b in range(NB):
                if b >= 2:
                    pe.wait_ge(s_rc, b - 1)
                project(pR[b % 2][:, 0:D], A[:, b, :], 1, 0).then_inc(s_rp, 1)
                if b == 1:
                    pe.wait_ge(s_dg, 1)
                    pe.matmul(pC[:, 0:P], ones[:, :], dg[:, 0, :], start=True, stop=True)
                    pe.matmul(pC[:, P:2 * P], ones[:, :], dg[:, 1, :], start=True, stop=True).then_inc(s_bc, 1)
                if 0 <= b - 2 < NGX - NGR:
                    turn(NGR + b - 2)
                if 0 <= b - 3 < NGX - NGR:
                    pool_features(NGR + b - 3)
                for k in hist_of(b):
                    histogram(k)
                if b == H0 + NB // 2 + 1:
                    pe.wait_ge(s_hc, 1)
                    pe.matmul(pC[:, 256:256 + NT], upper[:, :], deg[:, :], start=True, stop=True)
                    pe.matmul(pC[:, 384:384 + NT], ones[:, :], deg[:, :], start=True,
                              stop=True).then_inc(s_cum, 1)

            def carry(phase):
                pe.wait_ge(s_cmb, (phase + 1) * TS)
                last = TS - 1
                pe.transpose(pC[:, 0:P], S[:, last // T % NS, last % T, 0:D], ident[:, :]).then_inc(s_lt, 1)
                pe.wait_ge(s_cx, phase + 1)
                pe.transpose(pC[:, P:2 * P], CX[:, 0:P], ident[:, :]).then_inc(s_cp, 1)

            def node_stage(phase, read):
                for i in range(NGR + 1):
                    if i < NGR:
                        k = phase * NGR + i
                        pe.wait_ge(s_sc, k + 1)
                        if k >= 2:
                            pe.wait_ge(s_nt, k - 1)
                        for j in tiles_of(i):
                            ins = pe.transpose(pT[i % 2][:, j % GT, :], NR[:, i % NRS, j % GT, 0:D],
                                               ident[:, :])
                        ins.then_inc(s_mt, 1)
                    g = i - 1
                    if g >= 0:
                        pe.wait_ge(s_nt, phase * NGR + g + 1)
                        if g >= 2:
                            pe.wait_ge(read, g - 1)
                        for j in tiles_of(g):
                            ins = project(pM[g % 2][:, j % GT, :], NTT[:, g % 2, j % GT, :],
                                          (2, 4)[phase], None)
                        ins.then_inc(s_mm, 1)

            carry(0)
            node_stage(0, s_rst)
            pe.wait_ge(s_hn, NGR)
            for b in range(NB):
                pe.wait_ge(s_cmb, TS + steps_of(b)[0])
                if b >= 1:
                    pe.wait_ge(s_qh, b)
                pe.transpose(pR[0][:, 0:P], A[:, b, :], ident[:, :]).then_inc(s_qt, 1)
                pe.wait_ge(s_qh, b + 1)
                if b >= 1:
                    pe.wait_ge(s_qc, b)
                project(pR[1][:, 0:D], NTT[:, 0, b % 2, :], 3, 1).then_inc(s_qp, 1)
            carry(1)
            node_stage(1, s_y)


_NAMES = ["x", "src", "dstx", "ew", "w_pool", "b_pool", "w1s", "w1n", "b1", "w2s", "w2n", "b2"]


def kernel(x, src, dst, edge_attr_128, edge_weight, L0_gnn_W_pool, L0_gnn_b_pool, L0_gnn_W1_self,
           L0_gnn_W1_neigh, L0_gnn_b1, L0_gnn_W2_self, L0_gnn_W2_neigh, L0_gnn_b2):
    import numpy as np
    import concourse.bacc as bacc
    from concourse.bass_utils import run_bass_kernel_spmd

    def filled(a, before, n, value):
        a = np.asarray(a)
        o = np.full((n,) + a.shape[1:], value, a.dtype)
        o[before:before + a.shape[0]] = a
        return o

    dstx = filled(dst, 1, EP + 1, N)
    dstx[0] = -1
    given = [filled(x, 0, NP, 0), filled(src, 0, EP, 0), dstx, filled(edge_weight, 0, EP, 0),
             L0_gnn_W_pool, L0_gnn_b_pool, L0_gnn_W1_self, L0_gnn_W1_neigh, L0_gnn_b1,
             L0_gnn_W2_self, L0_gnn_W2_neigh, L0_gnn_b2]
    nc = bacc.Bacc("TRN2", target_bir_lowering=False, num_devices=1)
    arrays, args = {}, []
    for name, a in zip(_NAMES, given):
        a = np.ascontiguousarray(np.asarray(a))
        arrays[f"in_{name}"] = a
        args.append(nc.dram_tensor(f"in_{name}", a.shape, mybir.dt.from_np(a.dtype), kind="ExternalInput").ap())
    out = nc.dram_tensor("out_0", (NP, D), F32, kind="ExternalOutput").ap()
    build(nc, *args, out)
    r = run_bass_kernel_spmd(nc, [arrays], core_ids=[0])
    return r.results[0]["out_0"][:N]
```
